# Optimizing a Trainium2 kernel written in Bass

```python
import numpy as np
import jax
import jax.numpy as jnp

def _softmax(x, axis=-1):
    return jax.nn.softmax(x, axis=axis)

def _gelu(x):
    return jax.nn.gelu(x, approximate=True)

def _silu(x):
    return jax.nn.silu(x)

def _sigmoid(x):
    return jax.nn.sigmoid(x)

def _layernorm(x, axis=-1, eps=1e-05):
    m = jnp.mean(x, axis=axis, keepdims=True)
    v = jnp.var(x, axis=axis, keepdims=True)
    return (x - m) / jnp.sqrt(v + eps)

def _scatter_add(tgt, idx, src, axis=0):
    return tgt.at[idx].add(src)

def _segment_sum(src, seg, n):
    return jax.ops.segment_sum(src, seg, n)
kernel_name = 'mk_gps_d1_gnn_r16_367c94'

def setup_inputs(seed: int=0):
    np.random.seed(seed)
    _w = jnp.asarray

    def _rec_inputs():
        import jax
        import jax.numpy as jnp
        _gk = jax.random.key(seed)
        x = -0.0002117 + 1 * jax.random.normal(jax.random.fold_in(_gk, 1), (6250, 256), jnp.float32)
        src = jax.random.randint(jax.random.fold_in(_gk, 2), (100000,), 0, 6250, jnp.int32)
        dst = jax.random.randint(jax.random.fold_in(_gk, 3), (100000,), 0, 6250, jnp.int32)
        _o = jnp.argsort(dst, stable=True)
        src = src[_o]
        dst = dst[_o]
        edge_weight = jax.random.uniform(jax.random.fold_in(_gk, 12), (100000,), jnp.float32, 0.0, 0.999998)
        return (x, src, dst, edge_weight)
    x, src, dst, edge_weight = _rec_inputs()

    def _L0_gnn_setup():
        import jax, jax.numpy as jnp
        import numpy as np
        N_NODES = 6250
        N_EDGES = 18750
        D = 256
        EPS = 1e-05
        ALPHA = 0.5

        def gcn_residual(x, edge_index, edge_weight, W, b, gamma, beta):
            src, dst = (edge_index[0], edge_index[1])
            h = x @ W
            deg = jax.ops.segment_sum(edge_weight, dst, num_segments=N_NODES) + 1.0
            dinv = jax.lax.rsqrt(deg)
            norm = dinv[src] * edge_weight * dinv[dst]
            agg = jax.ops.segment_sum(norm[:, None] * h[src], dst, num_segments=N_NODES)
            agg = agg + (dinv * dinv)[:, None] * h
            h = agg + b
            mu = jnp.mean(h, axis=-1, keepdims=True)
            var = jnp.mean(jnp.square(h - mu), axis=-1, keepdims=True)
            h = (h - mu) * jax.lax.rsqrt(var + EPS) * gamma + beta
            h = ALPHA * h + (1.0 - ALPHA) * x
            return jax.nn.relu(h)
        key = jax.random.key(seed)
        ks = jax.random.split(key, 6)
        x = jax.random.normal(ks[0], (N_NODES, D), dtype=jnp.float32)
        edge_index = jax.random.randint(ks[1], (2, N_EDGES), 0, N_NODES, dtype=jnp.int32)
        edge_weight = jax.random.uniform(ks[2], (N_EDGES,), dtype=jnp.float32)
        W = jax.random.normal(ks[3], (D, D), dtype=jnp.float32) / np.float32(np.sqrt(D))
        b = 0.01 * jax.random.normal(ks[4], (D,), dtype=jnp.float32)
        gamma = jnp.ones((D,), dtype=jnp.float32)
        beta = jnp.zeros((D,), dtype=jnp.float32)
        return {'x': x, 'edge_index': edge_index, 'edge_weight': edge_weight, 'W': W, 'b': b, 'gamma': gamma, 'beta': beta}
    _L0_gnn_all = _L0_gnn_setup()
    _L0_gnn_in = {k: v for k, v in _L0_gnn_all.items() if k in ('W', 'b', 'gamma', 'beta')}
    del _L0_gnn_all

    def _L0_mix_setup():
        import jax, jax.numpy as jnp
        import numpy as np
        NUM_HEADS = 8
        key = jax.random.key(seed)
        ks = jax.random.split(key, 5)
        B, N, C = (8, 1024, 256)
        x = jax.random.normal(ks[0], (B, N, C), dtype=jnp.float32)
        Wq = jax.random.normal(ks[1], (C, C), dtype=jnp.float32) * 0.02
        Wkv = jax.random.normal(ks[2], (2 * C, C), dtype=jnp.float32) * 0.02
        Wproj = jax.random.normal(ks[3], (C, C), dtype=jnp.float32) * 0.02
        bproj = jnp.zeros((C,), dtype=jnp.float32)
        return {'x': x, 'Wq': Wq, 'Wkv': Wkv, 'Wproj': Wproj, 'bproj': bproj}
    _L0_mix_all = _L0_mix_setup()
    _L0_mix_in = {k: v for k, v in _L0_mix_all.items() if k in ('Wq', 'Wkv', 'Wproj', 'bproj')}
    del _L0_mix_all

    def _L0_ffn_setup():
        import jax, jax.numpy as jnp
        import numpy as np
        B, S, H, F, E, K = (8, 256, 256, 512, 16, 2)
        EPS = 1e-05
        key = jax.random.key(seed)
        ks = jax.random.split(key, 9)
        sc = 0.02
        return {'x': jax.random.normal(ks[0], (B, S, H), dtype=jnp.float32), 'gate_w': jax.random.normal(ks[1], (H, E), dtype=jnp.float32) * sc, 'gate_b': jnp.zeros((E,), dtype=jnp.float32), 'w1': jax.random.normal(ks[2], (E, H, F), dtype=jnp.float32) * sc, 'b1': jnp.zeros((E, F), dtype=jnp.float32), 'w2': jax.random.normal(ks[3], (E, F, H), dtype=jnp.float32) * sc, 'b2': jnp.zeros((E, H), dtype=jnp.float32), 'gamma': jnp.ones((H,), dtype=jnp.float32), 'beta': jnp.zeros((H,), dtype=jnp.float32)}
    _L0_ffn_all = _L0_ffn_setup()
    _L0_ffn_in = {k: v for k, v in _L0_ffn_all.items() if k in ('gate_w', 'gate_b', 'w1', 'b1', 'w2', 'b2', 'gamma', 'beta')}
    del _L0_ffn_all
    return {'x': x, 'src': src, 'dst': dst, 'edge_weight': edge_weight, 'L0_gnn_W': _L0_gnn_in['W'], 'L0_gnn_b': _L0_gnn_in['b'], 'L0_gnn_gamma': _L0_gnn_in['gamma'], 'L0_gnn_beta': _L0_gnn_in['beta'], 'L0_mix_Wq': _L0_mix_in['Wq'], 'L0_mix_Wkv': _L0_mix_in['Wkv'], 'L0_mix_Wproj': _L0_mix_in['Wproj'], 'L0_mix_bproj': _L0_mix_in['bproj'], 'L0_ffn_gate_w': _L0_ffn_in['gate_w'], 'L0_ffn_gate_b': _L0_ffn_in['gate_b'], 'L0_ffn_w1': _L0_ffn_in['w1'], 'L0_ffn_b1': _L0_ffn_in['b1'], 'L0_ffn_w2': _L0_ffn_in['w2'], 'L0_ffn_b2': _L0_ffn_in['b2'], 'L0_ffn_gamma': _L0_ffn_in['gamma'], 'L0_ffn_beta': _L0_ffn_in['beta']}

def reference(x, src, dst, edge_weight, L0_gnn_W, L0_gnn_b, L0_gnn_gamma, L0_gnn_beta, L0_mix_Wq, L0_mix_Wkv, L0_mix_Wproj, L0_mix_bproj, L0_ffn_gate_w, L0_ffn_gate_b, L0_ffn_w1, L0_ffn_b1, L0_ffn_w2, L0_ffn_b2, L0_ffn_gamma, L0_ffn_beta):
    import jax
    import jax.numpy as jnp

    def _L0_gnn_ref(x, edge_index, edge_weight, W, b, gamma, beta):
        import jax, jax.numpy as jnp
        import numpy as np
        N_NODES = 6250
        N_EDGES = 18750
        D = 256
        EPS = 1e-05
        ALPHA = 0.5

        def gcn_residual(x, edge_index, edge_weight, W, b, gamma, beta):
            src, dst = (edge_index[0], edge_index[1])
            h = x @ W
            deg = jax.ops.segment_sum(edge_weight, dst, num_segments=N_NODES) + 1.0
            dinv = jax.lax.rsqrt(deg)
            norm = dinv[src] * edge_weight * dinv[dst]
            agg = jax.ops.segment_sum(norm[:, None] * h[src], dst, num_segments=N_NODES)
            agg = agg + (dinv * dinv)[:, None] * h
            h = agg + b
            mu = jnp.mean(h, axis=-1, keepdims=True)
            var = jnp.mean(jnp.square(h - mu), axis=-1, keepdims=True)
            h = (h - mu) * jax.lax.rsqrt(var + EPS) * gamma + beta
            h = ALPHA * h + (1.0 - ALPHA) * x
            return jax.nn.relu(h)
        return gcn_residual(x, edge_index, edge_weight, W, b, gamma, beta)

    def _L0_mix_ref(x, Wq, Wkv, Wproj, bproj):
        import jax, jax.numpy as jnp
        import numpy as np
        NUM_HEADS = 8
        B, N, C = x.shape
        h = NUM_HEADS
        d = C // h
        q = jnp.einsum('bnc,oc->bno', x, Wq).reshape(B, N, h, d).transpose(0, 2, 1, 3)
        kv = jnp.einsum('bnc,oc->bno', x, Wkv).reshape(B, N, 2, h, d)
        k = kv[:, :, 0].transpose(0, 2, 1, 3)
        v = kv[:, :, 1].transpose(0, 2, 1, 3)
        q = jax.nn.elu(q) + 1.0
        k = jax.nn.elu(k) + 1.0
        k_sum = k.sum(axis=2)
        D_inv = 1.0 / jnp.maximum(jnp.einsum('bhnd,bhd->bhn', q, k_sum), 1e-06)
        context = jnp.einsum('bhnd,bhne->bhde', k, v)
        attn = jnp.einsum('bhnd,bhde->bhne', q, context) * D_inv[..., None]
        out = attn.transpose(0, 2, 1, 3).reshape(B, N, C)
        out = jnp.einsum('bnc,oc->bno', out, Wproj) + bproj
        return out

    def _L0_ffn_ref(x, gate_w, gate_b, w1, b1, w2, b2, gamma, beta):
        import jax, jax.numpy as jnp
        import numpy as np
        B, S, H, F, E, K = (8, 256, 256, 512, 16, 2)
        EPS = 1e-05
        gate_logits = x @ gate_w + gate_b
        topk_vals, topk_idx = jax.lax.top_k(gate_logits, K)
        topk_w = jax.nn.softmax(topk_vals, axis=-1)
        h = jax.nn.relu(jnp.einsum('bsh,ehf->bsef', x, w1) + b1)
        expert_out = jnp.einsum('bsef,efh->bseh', h, w2) + b2
        sel = jnp.take_along_axis(expert_out, topk_idx[:, :, :, None], axis=2)
        moe = jnp.sum(topk_w[..., None] * sel, axis=2)
        y = x + moe
        mu = jnp.mean(y, axis=-1, keepdims=True)
        var = jnp.var(y, axis=-1, keepdims=True)
        return (y - mu) / jnp.sqrt(var + EPS) * gamma + beta
    edge_index = jnp.stack([src, dst])
    xn = _layernorm(x, axis=-1)
    x = x + _L0_gnn_ref(xn, edge_index, edge_weight, L0_gnn_W, L0_gnn_b, L0_gnn_gamma, L0_gnn_beta) + _L0_mix_ref(xn[None], L0_mix_Wq, L0_mix_Wkv, L0_mix_Wproj, L0_mix_bproj)[0]
    x = x + _L0_ffn_ref(_layernorm(x, axis=-1)[None], L0_ffn_gate_w, L0_ffn_gate_b, L0_ffn_w1, L0_ffn_b1, L0_ffn_w2, L0_ffn_b2, L0_ffn_gamma, L0_ffn_beta)[0]
    return x

_drawn_inputs = setup_inputs


def setup_inputs(seed=0):
    import zlib

    import numpy as np

    out = dict(_drawn_inputs(seed))
    spreads = {'L0_gnn_gamma': (1.0, 0.2),
     'L0_gnn_beta': (0.0, 0.282),
     'L0_mix_bproj': (0.0, 0.1),
     'L0_ffn_gate_b': (0.0, 0.27),
     'L0_ffn_b1': (0.0, 0.8),
     'L0_ffn_b2': (0.0, 0.1),
     'L0_ffn_gamma': (1.0, 0.2),
     'L0_ffn_beta': (0.0, 0.1)}
    factors = {'L0_gnn_b': 5.678, 'L0_mix_Wq': 8.0, 'L0_mix_Wkv': 8.0, 'L0_mix_Wproj': 8.0}
    for name, (base, spread) in spreads.items():
        noise = np.random.default_rng([zlib.crc32(name.encode()), seed]).standard_normal(out[name].shape)
        drawn = base * np.exp(spread * noise) if base else spread * noise
        out[name] = jnp.asarray(drawn.astype(out[name].dtype))
    for name, factor in factors.items():
        out[name] = (out[name] * factor).astype(out[name].dtype)
    return out
```

```python
from contextlib import ExitStack

import numpy as np

import concourse.bass as bass
from concourse import mybir

F32 = mybir.dt.float32
BF16 = mybir.dt.bfloat16
F16 = mybir.dt.float16
I32 = mybir.dt.int32
ALU = mybir.AluOpType
ACT = mybir.ActivationFunctionType
AX = mybir.AxisListType

P = 128
N = 6250
D = 256
DC = D // P
NT = -(-N // P)
NP = NT * P
NE = 100000
NB = 784
SUB = NB // NT // 2
NEP = NB * P
H = 8
HC = H // DC
HD = D // H
E = 16
F = 512
FC = F // P
BLOCK = 2 * P
BLOCKS = 2 * NP // BLOCK + E
GROUP = 16
PAIRS = NB // 2
EPS = 1e-5
CHAIN_COMBINE = 42
CHAIN_TILE = 28

C_ID, C_TRI, C_IOTA, C_ONE = 0, P, 2 * P, 3 * P
C_VALID = 4 * P
C_POW = C_VALID + NT
C_TILE = C_POW + 1
C_DOWN = C_TILE + NT
C_N = C_DOWN + E
V_B, V_GAMMA, V_BETA, V_BPROJ, V_FGAMMA, V_FBETA, V_GATEB = (D * k for k in range(7))
V_N = V_GATEB + E
W_KV, W_Q, W_PROJ, W_GCN, W_GATE = 0, 2 * D, 3 * D, 4 * D, 5 * D
W_N = W_GATE + E


class Names:
    pass


class Count:

    def __init__(self, eng, sem, base, per_turn=None):
        self.eng, self.sem, self.base, self.n, self.per_turn = eng, sem, base, 0, per_turn

    def add(self, instruction):
        instruction.then_inc(self.sem, 1)
        self.n += 1
        return instruction

    def wait(self):
        self.eng.wait_ge(self.sem, self.base + self.n)

    def end(self):
        assert self.per_turn is None or self.n == self.per_turn, self.n


def memory(nc, ctx):
    def sb(name, shape, dt=F32):
        return ctx.enter_context(nc.sbuf_tensor(name, shape, dt))

    m = Names()
    m.const = sb("const", [P, C_N])
    m.vecs = sb("vecs", [P, V_N])
    m.weights = sb("weights", [P, DC, W_N])
    m.xn = sb("xn", [P, NT, D])
    m.x1 = sb("x1", [P, NT, D])
    m.dinv = sb("dinv", [P, NT])
    m.context = sb("context", [P, DC, P + HC])
    m.src = sb("src", [P, NB], I32)
    m.dst = sb("dst", [P, NB])
    m.w = sb("w", [P, NB])
    m.before = sb("before", [P, 64])
    m.flag = sb("flag", [1, 1], I32)
    m.logits = sb("logits", [P, NT, E])
    m.share = sb("share", [P, NT, 2])
    m.places = sb("places", [P, NT, 2], I32)
    m.lists = sb("lists", [1, 2, E], I32)
    m.pairs = sb("pairs", [1, 4, NT], I32)
    m.ident = m.const[:, C_ID:C_ID + P]
    m.tri = m.const[:, C_TRI:C_TRI + P]
    m.iota = m.const[:, C_IOTA:C_IOTA + P]
    m.ones = m.const[:, C_ONE:C_ONE + P]
    m.ps = [ctx.enter_context(nc.psum_tensor(f"bank{i}", [P, 512], F32)) for i in range(8)]
    m.spare = ctx.enter_context(nc.semaphore("spare"))
    return m


def tile(buf, t):
    return buf[:, bass.ds(t, 1), :].rearrange("p a d -> p (a d)")


def summed(dve, c, here, there, n):
    step = 1
    while step < n:
        c.wait()
        c.add(dve.tensor_copy(there[:, 0:step], here[:, 0:step]))
        c.add(dve.tensor_tensor(there[:, step:n], here[:, step:n], here[:, 0:n - step], ALU.add))
        here, there = there, here
        step *= 2
    c.wait()
    return here


def settle(eng, m):
    eng.sem_inc(m.spare, 1)


def prepare(nc, m, a):
    with ExitStack() as ctx:
        def sb(name, shape, dt=F32):
            return ctx.enter_context(nc.sbuf_tensor(name, shape, dt))

        def sem(name):
            return ctx.enter_context(nc.semaphore(name))

        ROWS = NB // 7
        dst_i = sb("dst_i", [P, NB], I32)
        part_i = sb("part_i", [P, 2, NB], I32)
        lo = sb("lo", [P, NB], F16)
        hi = sb("hi", [P, NB], F16)
        w_parts = sb("w_parts", [P, 3, NB], F16)
        w_rest = sb("w_rest", [P, NB])
        seq = sb("seq", [ROWS, 2, 7 * P], I32)
        seq_f = sb("seq_f", [ROWS, 7 * P])
        drops = sb("drops", [P, 1])
        stats = sb("stats", [P, NT, 6])
        mean = sb("mean", [P, NT])
        std = sb("std", [P, NT])
        rstd = sb("rstd", [P, NT])
        cur = sb("cur", [P, D])
        xnT = sb("xnT", [P, DC, P])
        ek = sb("ek", [P, D])
        rk = sb("rk", [P, D])
        kk = sb("kk", [P, D])
        vv = sb("vv", [P, DC, P + 1])
        iota_x = sb("iota_x", [P, P, SUB], F16)
        hot_lo = sb("hot_lo", [P, 2, P, SUB], F16)
        hot_hi = sb("hot_hi", [P, 2, NT, SUB], F16)
        hot_w = sb("hot_w", [P, 2, 3, NT, SUB], F16)
        zero = sb("zero", [P, 3 * NT])
        xs = sb("xs", [P, 7, D])
        deg = sb("deg", [P, 3, NT])
        t_i = sb("t_i", [P, 2, 64], I32)
        tf = [sb(f"tf{k}", [P, 64]) for k in range(6)]
        table_f = sb("table_f", [1, 4, NT])
        fill = sb("fill", [P, 2, D])

        ld_const, ld_x, ld_edge, ld_w, ld_x1, ld_seq = map(sem, ("ld_const", "ld_x", "ld_edge", "ld_w", "ld_x1", "ld_seq"))
        fill_ok, zeroed, stats_ok, var_ok, rstd_ok, normed, cur_ok = map(sem, (
            "fill_ok", "zeroed", "stats_ok", "var_ok", "rstd_ok", "normed", "cur_ok"))
        tr_ok, xnT_ok, kv_ok, exp_ok, vcopy, v_ok, kmin, k_ok, ctx_mm = map(sem, (
            "tr_ok", "xnT_ok", "kv_ok", "exp_ok", "vcopy", "v_ok", "kmin", "k_ok", "ctx_mm"))
        hot_ok, hot_hi_ok, deg_mm, deg_ok, dinv_ok, sums_ok, dchain = map(sem, (
            "hot_ok_p", "hot_hi_ok", "deg_mm", "deg_ok", "dinv_ok", "sums_ok", "dchain"))
        filled = [sem("filled0"), sem("filled1")]
        xs_ok = [sem("xs_ok0"), sem("xs_ok1")]
        xs_sent = [sem("xs_sent0"), sem("xs_sent1")]

        tr_ps = m.ps[0][:, 0:D].rearrange("p (c n) -> p c n", c=DC)
        kv_ps = m.ps[1]
        deg_ps = m.ps[2][:, 0:3 * NT].rearrange("p (a t) -> p a t", a=3)
        ctx_ps = [m.ps[4][:, 0:P + 1], m.ps[5][:, 0:P + 1]]
        sums_ps = m.ps[6][:, 0:NT]
        drops_ps = m.ps[6][:, 64:65]
        HALVES = ((0, 4), (4, 7))
        table = a.table.rearrange("(t p) d -> p t d", p=P)
        block = ctx.enter_context(nc.Block())

        @block.sync
        def _(sp):
            sp.dma_start(dst_i[:], a.dst_cols).then_inc(ld_edge, 16)
            sp.dma_start(m.w[:], a.w_cols).then_inc(ld_edge, 16)
            sp.dma_start(m.const[:], a.const).then_inc(ld_const, 16)
            sp.dma_start(m.xn[:], a.x.rearrange("(t p) d -> p t d", p=P)).then_inc(ld_x, 16)
            sp.dma_start(m.weights[:], a.weights).then_inc(ld_w, 16)
            sp.dma_start(seq[:], a.dst_seq).then_inc(ld_seq, 16)
            sp.dma_start(m.vecs[:], a.vecs).then_inc(ld_w, 16)
            sp.dma_start(m.src[:], a.src_cols).then_inc(ld_w, 16)
            sp.dma_start(m.x1[:], a.x.rearrange("(t p) d -> p t d", p=P)).then_inc(ld_x1, 16)
            sp.wait_ge(fill_ok, 1)
            with sp.Fori(0, BLOCKS) as b:
                for j, buf in enumerate((a.lists_in, a.lists_out)):
                    sp.dma_start(buf[bass.ds(b * BLOCK, BLOCK), :].rearrange("(p k) d -> p k d", k=2), fill[:]
                                 ).then_inc(filled[j], 16)
            with sp.Fori(0, NT // 7) as g:
                for part, (j0, j1) in enumerate(HALVES):
                    sp.wait_ge(xs_ok[part], g + 1)
                    sp.dma_start(table[:, bass.ds(g * 7 + j0, j1 - j0), :], xs[:, j0:j1, :]).then_inc(xs_sent[part], 16)
            for part in range(2):
                sp.wait_ge(filled[part], 16 * BLOCKS)
                sp.wait_ge(xs_sent[part], 16 * (NT // 7))
            sp.wait_ge(ld_x1, 16)
            sp.wait_ge(ld_w, 48)

        @block.vector
        def _(dve):
            c = Count(dve, dchain, 0)
            dve.memset(fill[:], 0.0).then_inc(fill_ok, 1)
            c.add(dve.memset(m.context[:], 0.0))
            c.add(dve.memset(drops[:], 0.0))
            dve.memset(zero[:], 0.0).then_inc(zeroed, 1)
            dve.wait_ge(ld_edge, 32)
            c.add(dve.tensor_single_scalar(part_i[:, 0, :], dst_i[:], P - 1, ALU.bitwise_and))
            c.add(dve.tensor_single_scalar(part_i[:, 1, :], dst_i[:], 7, ALU.arith_shift_right))
            c.add(dve.tensor_copy(m.dst[:], dst_i[:]))
            c.add(dve.tensor_copy(w_parts[:, 0, :], m.w[:]))
            c.add(dve.memset(w_parts[:, 2, :], 1.0))
            c.wait()
            c.add(dve.tensor_copy(lo[:], part_i[:, 0, :]))
            c.add(dve.tensor_copy(hi[:], part_i[:, 1, :]))
            c.add(dve.tensor_tensor(w_rest[:], m.w[:], w_parts[:, 0, :], ALU.subtract))
            dve.wait_ge(ld_const, 16)
            c.add(dve.tensor_copy(iota_x[:], m.iota[:, :, None].broadcast_to([P, P, SUB])))
            c.wait()
            c.add(dve.tensor_copy(w_parts[:, 1, :], w_rest[:]))
            c.wait()
            dve.wait_ge(ld_x, 16)
            with dve.Fori(0, NT) as t:
                dve.bn_stats(tile(stats, t), tile(m.xn, t)).then_inc(stats_ok, 1)
            dve.wait_ge(stats_ok, NT)
            c.add(dve.tensor_tensor(mean[:], stats[:, :, 1], stats[:, :, 4], ALU.add))
            c.add(dve.tensor_tensor(rstd[:], stats[:, :, 1], stats[:, :, 4], ALU.subtract))
            c.add(dve.tensor_tensor(std[:], stats[:, :, 2], stats[:, :, 5], ALU.add))
            c.wait()
            c.add(dve.tensor_scalar(mean[:], mean[:], 0.5, None, ALU.mult))
            c.add(dve.tensor_tensor(rstd[:], rstd[:], rstd[:], ALU.mult))
            c.add(dve.tensor_scalar(std[:], std[:], 1.0 / D, EPS, ALU.mult, ALU.add))
            c.wait()
            dve.scalar_tensor_tensor(std[:], rstd[:], 0.25, std[:], ALU.mult, ALU.add).then_inc(var_ok, 1)
            dve.wait_ge(rstd_ok, 1)
            with dve.Fori(0, NT) as t:
                row = tile(m.xn, t)
                dve.tensor_scalar(row, row, mean[:, bass.ds(t, 1)], rstd[:, bass.ds(t, 1)], ALU.subtract, ALU.mult
                                  ).then_inc(normed, 1)
            with dve.Fori(0, NT) as t:
                for k in range(2):
                    b = (t * 2 + k) * SUB
                    hi_c = hi[:, bass.ds(b, SUB)]
                    dve.wait_ge(deg_mm, t * 2 + k + 1)
                    dve.tensor_tensor(hot_lo[:, k], iota_x[:], lo[:, bass.ds(b, SUB)][:, None, :].broadcast_to([P, P, SUB]),
                                      ALU.is_equal)
                    dve.tensor_tensor(hot_hi[:, k], iota_x[:, 0:NT, :], hi_c[:, None, :].broadcast_to([P, NT, SUB]),
                                      ALU.is_equal).then_inc(hot_hi_ok, 1)
                    dve.wait_ge(hot_hi_ok, t * 2 + k + 1)
                    dve.tensor_tensor(hot_w[:, k], hot_hi[:, k, None, :, :].broadcast_to([P, 3, NT, SUB]),
                                      w_parts[:, :, bass.ds(b, SUB)][:, :, None, :].broadcast_to([P, 3, NT, SUB]),
                                      ALU.mult).then_inc(hot_ok, 1)
            dve.wait_ge(ld_seq, 16)
            c.add(dve.tensor_single_scalar(seq[:], seq[:], 7, ALU.arith_shift_right))
            c.wait()
            c.add(dve.tensor_tensor(seq_f[:], seq[:, 0, :], seq[:, 1, :], ALU.is_gt))
            c.wait()
            c.add(dve.reduce_sum(drops[0:ROWS, :], seq_f[:], axis=AX.X))
            dve.wait_ge(deg_mm, 2 * NT + 3)
            c.add(dve.tensor_copy(deg[:], deg_ps))
            c.wait()
            c.add(dve.tensor_tensor(std[:], deg[:, 0, :], deg[:, 1, :], ALU.add))
            c.wait()
            dve.tensor_scalar(std[:], std[:], 1.0, None, ALU.add).then_inc(deg_ok, 1)
            dve.wait_ge(dinv_ok, 1)

            def scaled(g, first):
                for part, (j0, j1) in enumerate(HALVES):
                    if not first:
                        dve.wait_ge(xs_sent[part], g * 16)
                    for j in range(j0, j1):
                        last = dve.tensor_scalar(xs[:, j, :], tile(m.xn, g * 7 + j), m.dinv[:, bass.ds(g * 7 + j, 1)], None, ALU.mult)
                    last.then_inc(xs_ok[part], 1)

            scaled(0, True)
            with dve.Fori(1, NT // 7) as g:
                scaled(g, False)
            dve.wait_ge(sums_ok, 1)
            c.add(dve.memset(tf[0][:], 0.0))
            c.add(dve.memset(tf[1][:], 0.0))
            c.wait()
            c.add(dve.tensor_copy(tf[0][:, 1:NT + 1], sums_ps))
            c.add(dve.tensor_copy(m.flag[:], drops_ps[0:1, :]))
            here = summed(dve, c, tf[0], tf[1], NT + 1)
            c.add(dve.tensor_copy(m.before[:], here[:]))
            c.add(dve.tensor_copy(t_i[:, 0, :], here[:]))
            c.add(dve.tensor_scalar(tf[2][:], here[:], 127.0, None, ALU.add))
            c.wait()
            c.add(dve.tensor_copy(t_i[:, 1, :], tf[2][:]))
            c.wait()
            c.add(dve.tensor_single_scalar(t_i[:], t_i[:], 7, ALU.arith_shift_right))
            c.wait()
            c.add(dve.tensor_copy(tf[2][:, 0:NT], t_i[:, 0, 0:NT]))
            c.add(dve.tensor_copy(tf[3][:, 0:NT], t_i[:, 1, 1:NT + 1]))
            c.wait()
            c.add(dve.scalar_tensor_tensor(tf[3][:, 0:NT], tf[2][:, 0:NT], 1.0, tf[3][:, 0:NT], ALU.add, ALU.max))
            c.wait()
            c.add(dve.tensor_scalar(tf[3][:, 0:NT], tf[3][:, 0:NT], 1.0, None, ALU.add))
            c.wait()
            c.add(dve.tensor_copy(t_i[:, 1, 0:NT], tf[3][:, 0:NT]))
            c.wait()
            c.add(dve.tensor_single_scalar(t_i[:], t_i[:], 1, ALU.arith_shift_right))
            c.wait()
            c.add(dve.tensor_copy(tf[2][:, 0:NT], t_i[:, 0, 0:NT]))
            c.add(dve.tensor_copy(tf[3][:, 0:NT], t_i[:, 1, 0:NT]))
            c.add(dve.memset(tf[4][:, 0:1], 0.0))
            c.wait()
            c.add(dve.tensor_tensor(tf[4][:, 1:NT], tf[3][:, 0:NT - 1], tf[2][:, 0:NT - 1], ALU.subtract))
            here = summed(dve, c, tf[4], tf[5], NT)
            c.add(dve.tensor_copy(table_f[0:1, 0, :], tf[2][0:1, 0:NT]))
            c.add(dve.tensor_copy(table_f[0:1, 1, :], tf[3][0:1, 0:NT]))
            c.add(dve.tensor_tensor(table_f[0:1, 2, :], here[0:1, 0:NT], tf[2][0:1, 0:NT], ALU.subtract))
            c.add(dve.memset(table_f[0:1, 3, NT - 1:NT], float(PAIRS)))
            c.add(dve.tensor_copy(table_f[0:1, 3, 0:NT - 1], tf[2][0:1, 1:NT]))
            c.wait()
            c.add(dve.tensor_copy(m.pairs[:], table_f[:]))
            dve.wait_ge(ctx_mm, NT + 2)
            for ch in range(DC):
                for h in range(HC):
                    r = slice(h * HD, (h + 1) * HD)
                    dve.tensor_copy(m.context[r, ch, r], ctx_ps[ch][r, r])
                    dve.tensor_copy(m.context[r, ch, P + h:P + h + 1], ctx_ps[ch][r, P:P + 1])

        @block.scalar
        def _(act):
            act.wait_ge(ld_const, 16)
            with act.Fori(0, NT) as t:
                act.wait_ge(normed, t + 1)
                act.wait_ge(tr_ok, t + 1)
                settle(act, m)
                act.activation(cur[:], tile(m.xn, t), ACT.Copy).then_inc(cur_ok, 1)
                act.wait_ge(tr_ok, t + 2)
                act.activation(xnT[:], tr_ps, ACT.Copy).then_inc(xnT_ok, 1)
                act.wait_ge(kv_ok, t + 1)
                act.wait_ge(k_ok, t + 1)
                act.activation(rk[:], kv_ps[:, 0:D], ACT.Relu)
                act.activation(ek[:], kv_ps[:, 0:D], ACT.Exp).then_inc(exp_ok, 1)
                act.wait_ge(ctx_mm, t + 1)
                act.activation(vv[:, :, 0:P], kv_ps[:, D:2 * D].rearrange("p (c n) -> p c n", c=DC), ACT.Copy)
                settle(act, m)
                act.activation(vv[:, :, P:P + 1], m.const[:, bass.ds(C_VALID + t, 1)][:, :, None].broadcast_to([P, DC, 1]),
                               ACT.Copy).then_inc(v_ok, 1)

        @block.gpsimd
        def _(pool):
            pool.wait_ge(ld_const, 16)
            minus_half = m.const[:, C_POW:C_POW + 1].broadcast_to([P, NT])
            pool.wait_ge(var_ok, 1)
            pool.tensor_tensor(rstd[:], std[:], minus_half, ALU.pow).then_inc(rstd_ok, 1)
            with pool.Fori(0, NT) as t:
                pool.wait_ge(exp_ok, t + 1)
                settle(pool, m)
                pool.tensor_scalar(ek[:], ek[:], 1.0, None, ALU.min).then_inc(kmin, 1)
                pool.wait_ge(kmin, t + 1)
                pool.wait_ge(ctx_mm, t + 1)
                pool.tensor_tensor(kk[:], ek[:], rk[:], ALU.add).then_inc(k_ok, 1)
            pool.wait_ge(deg_ok, 1)
            pool.tensor_tensor(m.dinv[:], std[:], minus_half, ALU.pow).then_inc(dinv_ok, 1)

        @block.tensor
        def _(pe):
            pe.wait_ge(zeroed, 1)
            nc.tensor.matmul(m.ps[2][:, 0:3 * NT], zero[:, 0:P], zero[:], start=True, stop=False)
            for ch in range(DC):
                last = nc.tensor.matmul(ctx_ps[ch], zero[:, 0:P], zero[:, 0:P + 1], start=True, stop=False)
            last.then_inc(ctx_mm, 1)
            pe.sem_inc(deg_mm, 2)
            pe.sem_inc(tr_ok, 1)
            pe.sem_inc(k_ok, 1)
            pe.wait_ge(ld_const, 16)
            pe.wait_ge(ld_w, 48)

            def degrees(turn, slot):
                pe.wait_ge(hot_ok, turn + 1)
                for j in range(SUB):
                    last = nc.tensor.matmul(deg_ps, hot_lo[:, slot, :, j], hot_w[:, slot, :, :, j], start=False, stop=False)
                last.then_inc(deg_mm, 1)

            with pe.Fori(0, NT) as t:
                pe.wait_ge(cur_ok, t + 1)
                for ch in range(DC):
                    last = nc.tensor.transpose(tr_ps[:, ch, :], cur[:, ch * P:(ch + 1) * P], m.ident)
                last.then_inc(tr_ok, 1)
                degrees(t * 2, 0)
                pe.wait_ge(xnT_ok, t + 1)
                for ch in range(DC):
                    last = nc.tensor.matmul(kv_ps[:], xnT[:, ch, :], m.weights[:, ch, W_KV:W_KV + 2 * D],
                                            start=(ch == 0), stop=(ch == DC - 1))
                last.then_inc(kv_ok, 1)
                degrees(t * 2 + 1, 1)
                pe.wait_ge(k_ok, t + 2)
                pe.wait_ge(v_ok, t + 1)
                for ch in range(DC):
                    last = nc.tensor.matmul(ctx_ps[ch], kk[:, ch * P:(ch + 1) * P], vv[:, ch, :], start=False, stop=False)
                last.then_inc(ctx_mm, 1)
            nc.tensor.matmul(m.ps[2][:, 0:3 * NT], zero[:, 0:P], zero[:], start=False, stop=True).then_inc(deg_mm, 1)
            for ch in range(DC):
                last = nc.tensor.matmul(ctx_ps[ch], zero[:, 0:P], zero[:, 0:P + 1], start=False, stop=True)
            last.then_inc(ctx_mm, 1)
            pe.wait_ge(deg_ok, 1)
            nc.tensor.matmul(sums_ps, m.ones, deg[:, 2, :], start=True, stop=True)
            nc.tensor.matmul(drops_ps, m.ones, drops[:], start=True, stop=True).then_inc(sums_ok, 1)


def regroup(nc, m, a):
    with ExitStack() as ctx:
        def sb(name, shape, dt=F32):
            return ctx.enter_context(nc.sbuf_tensor(name, shape, dt))

        def sem(name):
            return ctx.enter_context(nc.semaphore(name))

        CHAIN = 9
        edges = sb("edges_sb", [P, NB, 3])
        edge = sb("edge", [P, 3])
        hi_i = sb("hi_i", [P, NB], I32)
        hi = sb("hi_r", [P, NB])
        run = sb("run", [P, NT])
        oh = sb("oh", [P, NT])
        spot = sb("spot", [P, NT])
        pos = sb("pos", [P, 1])
        pos_i = sb("pos_i", [P, 3], I32)
        pos_f = sb("pos_f", [P, 2])
        at = sb("at_r", [P, 1], I32)

        edges_ok, edge_ok, oh_ok, rank_ok, at_ok, put, at_free, back, chain = map(sem, (
            "edges_ok", "edge_ok", "oh_ok", "rank_ok_r", "at_ok_r", "put", "at_free", "back_r", "chain_r"))
        rank_ps, total_ps = m.ps[0][:, 0:NT], m.ps[1][:, 0:NT]
        block = ctx.enter_context(nc.Block())

        def out_of_order(eng):
            return eng.value_load(m.flag[0:1, 0:1], min_val=0, max_val=NE) > 0

        @block.vector
        def _(dve):
            with dve.If(out_of_order(dve)):
                dve.tensor_copy(edges[:, :, 0], m.src[:]).then_inc(edges_ok, 1)
                dve.tensor_copy(edges[:, :, 1], m.dst[:]).then_inc(edges_ok, 1)
                dve.tensor_copy(edges[:, :, 2], m.w[:]).then_inc(edges_ok, 1)
                c = Count(dve, chain, 0)
                c.add(dve.tensor_copy(run[:], m.before[:, 0:NT]))
                c.add(dve.tensor_copy(hi_i[:], m.dst[:]))
                c.wait()
                c.add(dve.tensor_single_scalar(hi_i[:], hi_i[:], 7, ALU.arith_shift_right))
                c.wait()
                c.add(dve.tensor_copy(hi[:], hi_i[:]))
                c.wait()
                start = c.n
                with dve.Fori(0, NB) as b:
                    c = Count(dve, chain, start + b * CHAIN, CHAIN)
                    c.wait()
                    dve.tensor_scalar(oh[:], m.iota[:, 0:NT], hi[:, bass.ds(b, 1)], None, ALU.is_equal).then_inc(oh_ok, 1)
                    dve.wait_ge(rank_ok, b + 1)
                    c.add(dve.tensor_tensor(spot[:], run[:], rank_ps, ALU.add))
                    c.wait()
                    c.add(dve.tensor_tensor(run[:], run[:], total_ps, ALU.add))
                    c.add(dve.tensor_tensor(spot[:], spot[:], oh[:], ALU.mult))
                    c.wait()
                    c.add(dve.reduce_sum(pos[:], spot[:], axis=AX.X))
                    c.wait()
                    c.add(dve.tensor_copy(pos_i[:, 0:1], pos[:]))
                    c.wait()
                    c.add(dve.tensor_single_scalar(pos_i[:, 1:2], pos_i[:, 0:1], P - 1, ALU.bitwise_and))
                    c.add(dve.tensor_single_scalar(pos_i[:, 2:3], pos_i[:, 0:1], 7, ALU.arith_shift_right))
                    c.wait()
                    c.add(dve.tensor_copy(pos_f[:], pos_i[:, 1:3]))
                    c.wait()
                    c.add(dve.scalar_tensor_tensor(pos[:], pos_f[:, 0:1], float(NB), pos_f[:, 1:2], ALU.mult, ALU.add))
                    c.wait()
                    dve.wait_ge(at_free, b + 1)
                    settle(dve, m)
                    dve.tensor_copy(at[:], pos[:]).then_inc(at_ok, 1)
                    c.end()
                dve.wait_ge(back, 16)
                dve.tensor_copy(m.src[:], edges[:, :, 0])
                dve.tensor_copy(m.dst[:], edges[:, :, 1])
                dve.tensor_copy(m.w[:], edges[:, :, 2])

        @block.tensor
        def _(pe):
            with pe.If(out_of_order(pe)):
                with pe.Fori(0, NB) as b:
                    pe.wait_ge(oh_ok, b + 1)
                    nc.tensor.matmul(rank_ps, m.tri, oh[:], start=True, stop=True)
                    nc.tensor.matmul(total_ps, m.ones, oh[:], start=True, stop=True).then_inc(rank_ok, 1)

        @block.gpsimd
        def _(pool):
            with pool.If(out_of_order(pool)):
                pool.sem_inc(at_free, 1)
                pool.wait_ge(edges_ok, 3)
                with pool.Fori(0, NB) as b:
                    pool.tensor_copy(edge[:], edges[:, bass.ds(b, 1), :].rearrange("p a d -> p (a d)")).then_inc(edge_ok, 1)
                    pool.wait_ge(edge_ok, b + 1)
                    pool.wait_ge(at_ok, b + 1)
                    settle(pool, m)
                    pool.indirect_dma_start(out=a.edges, in_=edge[:], in_offset=None,
                                            out_offset=bass.IndirectOffsetOnAxis(ap=at[:, 0:1], axis=0)).then_inc(put, 16)
                    pool.wait_ge(put, b * 16 + 16)
                    pool.sem_inc(at_free, 1)
                pool.dma_start(edges[:], a.edges.rearrange("(p b) d -> p b d", p=P)).then_inc(back, 16)
                pool.wait_ge(back, 16)


def layers(nc, m, a):
    with ExitStack() as ctx:
        def sb(name, shape, dt=F32):
            return ctx.enter_context(nc.sbuf_tensor(name, shape, dt))

        def sem(name):
            return ctx.enter_context(nc.semaphore(name))

        ring = sb("ring", [P, GROUP, D])
        staged = sb("staged", [P, 2, GROUP // 2], I32)
        hot = sb("hot", [P, 2, P])
        hot_self = sb("hot_self", [P, P])
        iota_t = sb("iota_t", [P, P])
        zeros = sb("zeros", [P, D], BF16)
        half = sb("half", [P, 2, D])
        ag = sb("ag", [P, D])
        agT = sb("agT", [P, DC, P])
        h = sb("h", [P, D])
        hn = sb("hn", [P, D])
        st = sb("st", [P, 2, 6])
        mv = sb("mv2", [P, 2, 2])
        var = sb("var", [P, 2])
        sd = sb("sd", [P, 2])
        rs = sb("rs", [P, 2])
        nt = sb("nt", [P, 2])
        cur = sb("cur_m", [P, D])
        xnT = sb("xnT_m", [P, DC, P])
        rq = sb("rq", [P, DC, P])
        eq = sb("eq", [P, DC, P])
        qT = sb("qT", [P, DC, P])
        den = sb("den", [P, DC, HC])
        att = sb("att", [P, DC, HC, HD])
        attT = sb("attT", [P, DC, P])
        x2 = sb("x2", [P, D])
        x2T = sb("x2T", [P, DC, P])

        landed = [sem(f"landed{j}") for j in range(GROUP)]
        gathered, freed, hot_free, staged_ok, hot_ok, self_ok, agg_ok, ag_ok, agtr_ok, agT_ok, gcn_ok = map(sem, (
            "gathered", "freed", "hot_free", "staged_ok", "hot_ok", "self_ok", "agg_ok", "ag_ok", "agtr_ok", "agT_ok", "gcn_ok"))
        cur_ok, curtr_ok, xnT_ok, q_ok, eq_ok, qT_ok, attn_ok, att_ok, atttr_ok, attT_ok, proj_ok = map(sem, (
            "cur_ok", "curtr_ok", "xnT_ok", "q_ok", "eq_ok", "qT_ok", "attn_ok", "att_ok", "atttr_ok", "attT_ok",
            "proj_ok"))
        var_ok, sd_ok, x2_ok, x2tr_ok, x2T_ok, gate_ok, chain, zeros_ok = map(sem, (
            "var_ok", "sd_ok", "x2_ok", "x2tr_ok", "x2T_ok", "gate_ok", "chain", "zeros_ok"))

        def chunks(bank):
            return m.ps[bank][:, 0:D].rearrange("p (c n) -> p c n", c=DC)

        agg_ps, proj_ps, gcn_ps, gate_ps = m.ps[0][:, 0:D], m.ps[4][:, 0:D], m.ps[6][:, 0:D], m.ps[7][:, D:D + E]
        curtr_ps, q_ps, agtr_ps, x2tr_ps = chunks(1), chunks(2), chunks(5), chunks(7)
        attn_ps = m.ps[3][:, 0:DC * (P + HC)].rearrange("p (c n) -> p c n", c=DC)
        block = ctx.enter_context(nc.Block())

        def of_tile(eng, row, t):
            return eng.value_load(m.pairs[0:1, row:row + 1, bass.ds(t, 1)].rearrange("p a b -> p (a b)"),
                                  min_val=(0, 1, 0, 0)[row], max_val=(PAIRS - 1, PAIRS, NT, PAIRS)[row])

        @block.sync
        def _(sp):
            with sp.Fori(0, NB // GROUP) as g:
                for j in range(GROUP):
                    sp.wait_ge(landed[j], g * 16 + 16)
                    sp.sem_inc(gathered, 1)

        @block.gpsimd
        def _(pool):
            HG = GROUP // 2

            def turn(g, first):
                for half_turn in range(2):
                    if not first:
                        pool.wait_ge(gathered, g * GROUP + half_turn * HG - HG)
                        settle(pool, m)
                    pool.tensor_copy(staged[:, half_turn, :], m.src[:, bass.ds(g * GROUP + half_turn * HG, HG)]
                                     ).then_inc(staged_ok, 1)
                    pool.wait_ge(staged_ok, g * 2 + half_turn + 1)
                    for j in range(half_turn * HG, half_turn * HG + HG):
                        if not first and j % 4 == 0:
                            pool.wait_ge(freed, g * (GROUP // 2) + (j + 4 - GROUP) // 2)
                            settle(pool, m)
                        pool.indirect_dma_start(
                            out=ring[:, j, :], out_offset=None, in_=a.table,
                            in_offset=bass.IndirectOffsetOnAxis(ap=staged[:, half_turn, j % HG:j % HG + 1], axis=0)
                        ).then_inc(landed[j], 16)

            turn(0, True)
            with pool.Fori(1, NB // GROUP) as g:
                turn(g, False)

        @block.vector
        def _(dve):
            c = Count(dve, chain, 0)
            c.add(dve.tensor_scalar(half[:], m.vecs[:, V_GAMMA:V_GAMMA + 2 * D].rearrange("p (a d) -> p a d", a=2),
                                    0.5, None, ALU.mult))
            dve.memset(zeros[:], 0.0).then_inc(zeros_ok, 1)
            start = c.n
            with dve.Fori(0, NT) as t:
                c = Count(dve, chain, start + t * CHAIN_TILE, CHAIN_TILE)
                pair0, pair_end, shared = (of_tile(dve, k, t) for k in range(3))
                c.wait()
                c.add(dve.tensor_scalar(iota_t[:], m.iota, m.const[:, bass.ds(C_TILE + t, 1)], None, ALU.add))
                dve.tensor_scalar(hot_self[:], m.ident, m.dinv[:, bass.ds(t, 1)], None, ALU.mult).then_inc(self_ok, 1)
                c.wait()
                settle(dve, m)
                with dve.Fori(pair0, pair_end) as pair:
                    for k in range(2):
                        dve.wait_ge(hot_free, (pair + shared) * 2 + k + 1)
                        dve.tensor_scalar(hot[:, k, :], iota_t[:], m.dst[:, bass.ds(pair * 2 + k, 1)],
                                          m.w[:, bass.ds(pair * 2 + k, 1)], ALU.is_equal, ALU.mult).then_inc(hot_ok, 1)

                dve.wait_ge(eq_ok, t + 1)
                dve.scalar_tensor_tensor(qT[:], eq[:], 1.0, rq[:], ALU.min, ALU.add).then_inc(qT_ok, 1)
                dve.wait_ge(gcn_ok, t + 1)
                c.add(dve.scalar_tensor_tensor(h[:], gcn_ps, m.dinv[:, bass.ds(t, 1)], m.vecs[:, V_B:V_B + D],
                                               ALU.mult, ALU.add))
                c.wait()
                c.add(dve.bn_stats(st[:, 0, :], h[:]))
                c.wait()
                settle(dve, m)
                c.add(dve.bn_aggr(mv[:, 0, :], st[:, 0, :]))
                c.wait()
                dve.tensor_scalar(var[:, 0:1], mv[:, 0, 1:2], EPS, None, ALU.add).then_inc(var_ok, 1)
                dve.wait_ge(attn_ok, t + 1)
                c.add(dve.tensor_scalar(den[:], attn_ps[:, :, P:P + HC], 1e-6, None, ALU.max))
                c.wait()
                c.add(dve.reciprocal(den[:], den[:]))
                c.wait()
                dve.tensor_tensor(att[:], attn_ps[:, :, 0:P].rearrange("p c (h d) -> p c h d", h=HC),
                                  den[:, :, :, None].broadcast_to([P, DC, HC, HD]), ALU.mult).then_inc(att_ok, 1)

                def newton(k):
                    c.add(dve.reciprocal(rs[:, k:k + 1], sd[:, k:k + 1]))
                    c.wait()
                    c.add(dve.tensor_tensor(nt[:, k:k + 1], rs[:, k:k + 1], rs[:, k:k + 1], ALU.mult))
                    c.wait()
                    c.add(dve.tensor_tensor(nt[:, k:k + 1], nt[:, k:k + 1], var[:, k:k + 1], ALU.mult))
                    c.wait()
                    c.add(dve.tensor_scalar(nt[:, k:k + 1], nt[:, k:k + 1], -0.5, 1.5, ALU.mult, ALU.add))
                    c.wait()
                    c.add(dve.tensor_tensor(rs[:, k:k + 1], rs[:, k:k + 1], nt[:, k:k + 1], ALU.mult))
                    c.wait()

                dve.wait_ge(sd_ok, t * 2 + 1)
                newton(0)
                c.add(dve.tensor_scalar(hn[:], h[:], mv[:, 0, 0:1], rs[:, 0:1], ALU.subtract, ALU.mult))
                c.wait()
                c.add(dve.tensor_tensor(hn[:], hn[:], half[:, 0, :], ALU.mult))
                c.wait()
                c.add(dve.tensor_tensor(hn[:], hn[:], half[:, 1, :], ALU.add))
                c.wait()
                c.add(dve.scalar_tensor_tensor(hn[:], tile(m.xn, t), 0.5, hn[:], ALU.mult, ALU.add))
                dve.wait_ge(proj_ok, t + 1)
                c.add(dve.tensor_tensor(h[:], proj_ps, m.vecs[:, V_BPROJ:V_BPROJ + D], ALU.add))
                c.wait()
                c.add(dve.scalar_tensor_tensor(h[:], hn[:], 0.0, h[:], ALU.max, ALU.add))
                c.wait()
                c.add(dve.tensor_tensor(h[:], h[:], tile(m.x1, t), ALU.add))
                c.wait()
                settle(dve, m)
                c.add(dve.tensor_copy(tile(m.x1, t), h[:]))
                c.add(dve.bn_stats(st[:, 1, :], h[:]))
                c.wait()
                settle(dve, m)
                c.add(dve.bn_aggr(mv[:, 1, :], st[:, 1, :]))
                c.wait()
                dve.tensor_scalar(var[:, 1:2], mv[:, 1, 1:2], EPS, None, ALU.add).then_inc(var_ok, 1)
                dve.wait_ge(sd_ok, t * 2 + 2)
                newton(1)
                dve.tensor_scalar(x2[:], h[:], mv[:, 1, 0:1], rs[:, 1:2], ALU.subtract, ALU.mult).then_inc(x2_ok, 1)
                c.add(dve.tensor_scalar(tile(m.xn, t), h[:], mv[:, 1, 0:1], rs[:, 1:2], ALU.subtract, ALU.mult))
                dve.wait_ge(gate_ok, t + 1)
                c.add(dve.tensor_tensor(tile(m.logits, t), gate_ps, m.vecs[:, V_GATEB:V_GATEB + E], ALU.add))
                c.end()

        @block.scalar
        def _(act):
            with act.Fori(0, NT) as t:
                act.wait_ge(curtr_ok, t + 1)
                settle(act, m)
                act.activation(cur[:], tile(m.xn, t), ACT.Copy).then_inc(cur_ok, 1)
                act.wait_ge(curtr_ok, t + 2)
                act.activation(xnT[:], curtr_ps, ACT.Copy).then_inc(xnT_ok, 1)
                act.wait_ge(q_ok, t + 1)
                act.wait_ge(qT_ok, t + 1)
                act.activation(rq[:], q_ps, ACT.Relu)
                act.activation(eq[:], q_ps, ACT.Exp).then_inc(eq_ok, 1)
                act.wait_ge(agg_ok, t + 1)
                act.activation(ag[:], agg_ps, ACT.Copy).then_inc(ag_ok, 1)
                act.wait_ge(agtr_ok, t + 1)
                act.activation(agT[:], agtr_ps, ACT.Copy).then_inc(agT_ok, 1)
                act.wait_ge(var_ok, t * 2 + 1)
                act.activation(sd[:, 0:1], var[:, 0:1], ACT.Sqrt).then_inc(sd_ok, 1)
                act.wait_ge(atttr_ok, t + 1)
                act.activation(attT[:], curtr_ps, ACT.Copy).then_inc(attT_ok, 1)
                act.wait_ge(var_ok, t * 2 + 2)
                act.activation(sd[:, 1:2], var[:, 1:2], ACT.Sqrt).then_inc(sd_ok, 1)
                act.wait_ge(x2tr_ok, t + 1)
                act.activation(x2T[:], x2tr_ps, ACT.Copy).then_inc(x2T_ok, 1)

        @block.tensor
        def _(pe):
            pe.wait_ge(zeros_ok, 1)
            pe.sem_inc(hot_free, 2)
            pe.sem_inc(curtr_ok, 1)
            pe.sem_inc(qT_ok, 1)

            def turned(to, of):
                for ch in range(DC):
                    last = nc.tensor.transpose(to[:, ch, :], of[:, ch * P:(ch + 1) * P], m.ident)
                return last

            def product(to, ofT, column, width):
                for ch in range(DC):
                    last = nc.tensor.matmul(to, ofT[:, ch, :], m.weights[:, ch, column:column + width],
                                            start=(ch == 0), stop=(ch == DC - 1))
                return last

            with pe.Fori(0, NT) as t:
                pair0, pair_end, shared, next0 = (of_tile(pe, k, t) for k in range(4))
                pe.wait_ge(cur_ok, t + 1)
                turned(curtr_ps, cur).then_inc(curtr_ok, 1)
                pe.wait_ge(xnT_ok, t + 1)
                for co in range(DC):
                    for ch in range(DC):
                        last = nc.tensor.matmul(q_ps[:, co, :], m.weights[:, ch, W_Q + co * P:W_Q + (co + 1) * P],
                                                xnT[:, ch, :], start=(ch == 0), stop=(ch == DC - 1))
                last.then_inc(q_ok, 1)
                pe.wait_ge(self_ok, t + 1)
                nc.tensor.matmul(agg_ps, hot_self[:], tile(m.xn, t), start=True, stop=False)
                with pe.Fori(pair0, pair_end) as pair:
                    for k in range(2):
                        pe.wait_ge(hot_ok, (pair + shared) * 2 + k + 1)
                        pe.wait_ge(gathered, pair * 2 + k + 1)
                        nc.tensor.matmul(agg_ps, hot[:, k, :], tile(ring, (pair * 2 + k) % GROUP), start=False, stop=False
                                         ).then_inc(hot_free, 1)
                    with pe.If(pair < next0):
                        nc.tensor.matmul(agg_ps[:, 0:1], zeros[:, 0:P], zeros[:, 0:1], start=False, stop=False
                                         ).then_inc(freed, 1)
                nc.tensor.matmul(agg_ps, zeros[:, 0:P], zeros[:], start=False, stop=True).then_inc(agg_ok, 1)
                pe.wait_ge(qT_ok, t + 2)
                for ch in range(DC):
                    last = nc.tensor.matmul(attn_ps[:, ch, :], qT[:, ch, :], m.context[:, ch, :], start=True, stop=True)
                last.then_inc(attn_ok, 1)
                pe.wait_ge(ag_ok, t + 1)
                turned(agtr_ps, ag).then_inc(agtr_ok, 1)
                pe.wait_ge(agT_ok, t + 1)
                product(gcn_ps, agT, W_GCN, D).then_inc(gcn_ok, 1)
                pe.wait_ge(att_ok, t + 1)
                turned(curtr_ps, att[:].rearrange("p c h d -> p (c h d)")).then_inc(atttr_ok, 1)
                pe.wait_ge(attT_ok, t + 1)
                product(proj_ps, attT, W_PROJ, D).then_inc(proj_ok, 1)
                pe.wait_ge(x2_ok, t + 1)
                turned(x2tr_ps, x2).then_inc(x2tr_ok, 1)
                pe.wait_ge(x2T_ok, t + 1)
                product(gate_ps, x2T, W_GATE, E).then_inc(gate_ok, 1)


def route(nc, m, a):
    with ExitStack() as ctx:
        def sb(name, shape, dt=F32):
            return ctx.enter_context(nc.sbuf_tensor(name, shape, dt))

        def sem(name):
            return ctx.enter_context(nc.semaphore(name))

        best = sb("best", [P, 2, NT])
        pick = sb("pick", [P, NT])
        score = sb("score", [P, NT, E])
        rest = sb("rest", [P, NT, E])
        one = [sb("one0", [P, NT, E]), sb("one1", [P, NT, E])]
        both = sb("both", [P, NT, E])
        pre = [sb("pre0", [P, NT, E]), sb("pre1", [P, NT, E])]
        gap = sb("gap", [P, NT])
        eg = sb("eg", [P, NT])
        place = sb("place", [P, NT])
        cnt = sb("cnt", [P, E])
        nb = sb("nb", [P, E])
        nb_i = sb("nb_i", [P, E], I32)
        b0 = [sb("b0a", [P, E]), sb("b0b", [P, E])]
        table = sb("table_e", [1, 2, E])
        rows = sb("rows", [P, 7, D])
        at = sb("at", [P, 7, 2], I32)

        chain, gap_ok, eg_ok, both_ok, rank_ok = map(sem, (
            "r_chain", "gap_ok", "eg_ok", "both_ok", "rank_ok"))
        rows_ok = [sem("rows_ok0"), sem("rows_ok1")]
        at_ok = [sem("at_ok0"), sem("at_ok1")]
        sent = [sem("sent0"), sem("sent1")]
        HALVES = ((0, 4), (4, 7))
        rank_ps = [m.ps[k][:, 0:25 * E].rearrange("p (t e) -> p t e", e=E) for k in (0, 1)]
        total_ps = [m.ps[k][:, 0:25 * E].rearrange("p (t e) -> p t e", e=E) for k in (2, 3)]
        SPLIT = ((0, 25), (25, NT))
        block = ctx.enter_context(nc.Block())

        @block.vector
        def _(dve):
            c = Count(dve, chain, 0)
            down = m.const[:, C_DOWN:C_DOWN + E][:, None, :].broadcast_to([P, NT, E])
            for k in range(2):
                of = (m.logits, rest)[k]
                c.add(dve.reduce_max(best[:, k, :], of[:], axis=AX.X))
                c.wait()
                c.add(dve.tensor_tensor(score[:], of[:], best[:, k, :, None].broadcast_to([P, NT, E]), ALU.is_equal))
                c.wait()
                c.add(dve.tensor_tensor(score[:], score[:], down, ALU.mult))
                c.wait()
                c.add(dve.reduce_max(pick[:], score[:], axis=AX.X))
                c.wait()
                c.add(dve.tensor_tensor(one[k][:], down, pick[:, :, None].broadcast_to([P, NT, E]), ALU.is_equal))
                c.wait()
                if k == 0:
                    c.add(dve.scalar_tensor_tensor(rest[:], one[0][:], -3e38, m.logits[:], ALU.mult, ALU.add))
                    c.wait()
            dve.tensor_tensor(both[:], one[0][:], one[1][:], ALU.add).then_inc(both_ok, 1)
            dve.tensor_tensor(gap[:], best[:, 1, :], best[:, 0, :], ALU.subtract).then_inc(gap_ok, 1)
            dve.wait_ge(eg_ok, 1)
            c.add(dve.tensor_scalar(gap[:], eg[:], 1.0, None, ALU.add))
            c.wait()
            c.add(dve.reciprocal(m.share[:, :, 0], gap[:]))
            c.wait()
            c.add(dve.tensor_tensor(m.share[:, :, 1], eg[:], m.share[:, :, 0], ALU.mult))
            dve.wait_ge(rank_ok, 1)
            c.add(dve.memset(pre[0][:, 0:1, :], 0.0))
            for k, (t0, t1) in enumerate(SPLIT):
                c.add(dve.tensor_copy(both[:, t0:t1, :], total_ps[k][:, 0:t1 - t0, :]))
            c.wait()
            c.add(dve.tensor_copy(pre[0][:, 1:NT, :], both[:, 0:NT - 1, :]))
            step, here, there = 1, pre[0], pre[1]
            while step < NT:
                c.wait()
                c.add(dve.tensor_copy(there[:, 0:step, :], here[:, 0:step, :]))
                c.add(dve.tensor_tensor(there[:, step:NT, :], here[:, step:NT, :], here[:, 0:NT - step, :], ALU.add))
                here, there = there, here
                step *= 2
            c.wait()
            c.add(dve.tensor_tensor(cnt[:], here[:, NT - 1, :], both[:, NT - 1, :], ALU.add))
            c.wait()
            c.add(dve.tensor_scalar(nb[:], cnt[:], 1.0, float(BLOCK - 1), ALU.max, ALU.add))
            c.wait()
            c.add(dve.tensor_copy(nb_i[:], nb[:]))
            c.wait()
            c.add(dve.tensor_single_scalar(nb_i[:], nb_i[:], BLOCK.bit_length() - 1, ALU.arith_shift_right))
            c.wait()
            c.add(dve.tensor_copy(nb[:], nb_i[:]))
            c.add(dve.memset(b0[0][:, 0:1], 0.0))
            c.wait()
            c.add(dve.tensor_copy(b0[0][:, 1:E], nb[:, 0:E - 1]))
            step, h0, h1 = 1, b0[0], b0[1]
            while step < E:
                c.wait()
                c.add(dve.tensor_copy(h1[:, 0:step], h0[:, 0:step]))
                c.add(dve.tensor_tensor(h1[:, step:E], h0[:, step:E], h0[:, 0:E - step], ALU.add))
                h0, h1 = h1, h0
                step *= 2
            c.wait()
            c.add(dve.tensor_copy(table[0:1, 0, :], h0[0:1, :]))
            c.add(dve.tensor_tensor(table[0:1, 1, :], h0[0:1, :], nb[0:1, :], ALU.add))
            c.add(dve.tensor_scalar(h1[:], h0[:], float(BLOCK), None, ALU.mult))
            c.wait()
            c.add(dve.tensor_copy(m.lists[:], table[:]))
            c.add(dve.tensor_tensor(here[:], here[:], h1[:, None, :].broadcast_to([P, NT, E]), ALU.add))
            c.wait()
            for k, (t0, t1) in enumerate(SPLIT):
                c.add(dve.tensor_tensor(here[:, t0:t1, :], here[:, t0:t1, :], rank_ps[k][:, 0:t1 - t0, :], ALU.add))
            c.wait()
            for k in range(2):
                c.add(dve.tensor_tensor(score[:], here[:], one[k][:], ALU.mult))
                c.wait()
                c.add(dve.reduce_sum(place[:], score[:], axis=AX.X))
                c.wait()
                c.add(dve.tensor_copy(m.places[:, :, k], place[:]))
                c.wait()
            for part, (j0, j1) in enumerate(HALVES):
                dve.tensor_copy(at[:, j0:j1, :], m.places[:, j0:j1, :]).then_inc(at_ok[part], 1)
            with dve.Fori(1, NT // 7) as g:
                for part, (j0, j1) in enumerate(HALVES):
                    dve.wait_ge(sent[part], g * (j1 - j0) * 32)
                    settle(dve, m)
                    dve.tensor_copy(at[:, j0:j1, :], m.places[:, bass.ds(g * 7 + j0, j1 - j0), :]).then_inc(at_ok[part], 1)

        @block.scalar
        def _(act):
            act.wait_ge(gap_ok, 1)
            act.activation(eg[:], gap[:], ACT.Exp).then_inc(eg_ok, 1)
            for part, (j0, j1) in enumerate(HALVES):
                act.activation(rows[:, j0:j1, :], m.xn[:, j0:j1, :], ACT.Copy).then_inc(rows_ok[part], 1)
            with act.Fori(1, NT // 7) as g:
                for part, (j0, j1) in enumerate(HALVES):
                    act.wait_ge(sent[part], g * (j1 - j0) * 32)
                    settle(act, m)
                    act.activation(rows[:, j0:j1, :], m.xn[:, bass.ds(g * 7 + j0, j1 - j0), :], ACT.Copy
                                   ).then_inc(rows_ok[part], 1)

        @block.tensor
        def _(pe):
            pe.wait_ge(both_ok, 1)
            for k, (t0, t1) in enumerate(SPLIT):
                nc.tensor.matmul(rank_ps[k][:, 0:t1 - t0, :], m.tri, both[:, t0:t1, :], start=True, stop=True)
                last = nc.tensor.matmul(total_ps[k][:, 0:t1 - t0, :], m.ones, both[:, t0:t1, :], start=True, stop=True)
            last.then_inc(rank_ok, 1)

        @block.gpsimd
        def _(pool):
            with pool.Fori(0, NT // 7) as g:
                for part, (j0, j1) in enumerate(HALVES):
                    pool.wait_ge(rows_ok[part], g + 1)
                    pool.wait_ge(at_ok[part], g + 1)
                    settle(pool, m)
                    for j in range(j0, j1):
                        for k in range(2):
                            pool.indirect_dma_start(out=a.lists_in, in_=rows[:, j, :], in_offset=None,
                                                    out_offset=bass.IndirectOffsetOnAxis(ap=at[:, j, k:k + 1], axis=0)
                                                    ).then_inc(sent[part], 16)
            for part, (j0, j1) in enumerate(HALVES):
                pool.wait_ge(sent[part], NT // 7 * (j1 - j0) * 32)


def experts(nc, m, a):
    with ExitStack() as ctx:
        def sb(name, shape, dt=F32):
            return ctx.enter_context(nc.sbuf_tensor(name, shape, dt))

        def sem(name):
            return ctx.enter_context(nc.semaphore(name))

        w1 = sb("w1", [P, 2, DC, F])
        w2 = sb("w2", [P, 2, FC, D])
        b1 = sb("b1", [P, FC, E])
        b2 = sb("b2", [P, 2, D])
        xin = sb("xin", [P, 2, D])
        xT = sb("xT", [P, DC, BLOCK])
        hT = sb("hT", [P, FC, BLOCK])
        y = sb("y", [P, 2, D])

        w_in = [sem("w_in0"), sem("w_in1")]
        b1_in, x_in, xtr_ok, xT_ok, up_ok, h_ok, down_ok, y_ok, y_out, done = map(sem, (
            "b1_in", "x_in", "xtr_ok", "xT_ok", "up_ok", "h_ok", "down_ok", "y_ok", "y_out", "done"))
        xtr_ps = m.ps[0][:].rearrange("p (c n) -> p c n", c=DC)
        up_ps = [m.ps[1 + fc][:, 0:BLOCK] for fc in range(FC)]
        down_ps = m.ps[5][:].rearrange("p (s d) -> p s d", s=2)
        block = ctx.enter_context(nc.Block())

        def of_list(eng, row, e):
            return eng.value_load(m.lists[0:1, row:row + 1, bass.ds(e, 1)].rearrange("p a b -> p (a b)"),
                                  min_val=(0, 1)[row], max_val=(BLOCKS - 1, BLOCKS)[row])

        def rows_of(buf, b):
            return buf[bass.ds(b * BLOCK, BLOCK), :].rearrange("(s p) d -> p s d", p=P)

        @block.gpsimd
        def _(pool):
            def load(e, slot):
                pool.dma_start(w1[:, slot], a.w1[bass.ds(e, 1)].rearrange("a (c p) f -> p (a c) f", p=P)).then_inc(w_in[slot], 16)
                pool.dma_start(w2[:, slot], a.w2[bass.ds(e, 1)].rearrange("a (c p) d -> p (a c) d", p=P)).then_inc(w_in[slot], 16)
                pool.dma_start(b2[:, slot], a.b2[bass.ds(e, 1)].rearrange("a p d -> p (a d)")).then_inc(w_in[slot], 16)

            load(0, 0)
            load(1, 1)
            with pool.Fori(1, E // 2) as i:
                for slot in range(2):
                    pool.wait_ge(done, i * 2 + slot - 1)
                    settle(pool, m)
                    load(i * 2 + slot, slot)

        @block.sync
        def _(sp):
            sp.dma_start(b1[:], a.b1).then_inc(b1_in, 16)
            sp.sem_inc(xtr_ok, 1)
            sp.sem_inc(y_out, 16)
            with sp.Fori(0, E) as e:
                first, end = of_list(sp, 0, e), of_list(sp, 1, e)
                with sp.Fori(first, end) as b:
                    sp.wait_ge(xtr_ok, b + 1)
                    sp.dma_start(xin[:], rows_of(a.lists_in, b)
                                 ).then_inc(x_in, 16)

        @block.scalar
        def _(act):
            with act.Fori(0, E) as e:
                first, end = of_list(act, 0, e), of_list(act, 1, e)
                with act.Fori(first, end) as b:
                    act.wait_ge(xtr_ok, b + 2)
                    act.activation(xT[:], xtr_ps, ACT.Copy).then_inc(xT_ok, 1)
                    for fc in range(FC):
                        act.wait_ge(up_ok, b * FC + fc + 1)
                        settle(act, m)
                        act.activation(hT[:, fc, :], up_ps[fc], ACT.Relu, bias=b1[:, fc, bass.ds(e, 1)]).then_inc(h_ok, 1)
                    act.wait_ge(y_ok, b + 1)
                    act.dma_start(rows_of(a.lists_out, b), y[:]
                                  ).then_inc(y_out, 16)
                    act.wait_ge(y_out, b * 16 + 32)

        @block.tensor
        def _(pe):
            with pe.Fori(0, E // 2) as i:
                for slot in range(2):
                    e = i * 2 + slot
                    first, end = of_list(pe, 0, e), of_list(pe, 1, e)
                    pe.wait_ge(w_in[slot], i * 48 + 48)
                    settle(pe, m)
                    with pe.Fori(first, end) as b:
                        pe.wait_ge(x_in, b * 16 + 16)
                        for s in range(2):
                            for ch in range(DC):
                                last = nc.tensor.transpose(xtr_ps[:, ch, s * P:(s + 1) * P], xin[:, s, ch * P:(ch + 1) * P], m.ident)
                        last.then_inc(xtr_ok, 1)
                        pe.wait_ge(xT_ok, b + 1)
                        for fc in range(FC):
                            for ch in range(DC):
                                last = nc.tensor.matmul(up_ps[fc], w1[:, slot, ch, fc * P:(fc + 1) * P], xT[:, ch, :],
                                                        start=(ch == 0), stop=(ch == DC - 1))
                            last.then_inc(up_ok, 1)
                        for s in range(2):
                            for fc in range(FC):
                                if s == 0:
                                    pe.wait_ge(h_ok, b * FC + fc + 1)
                                last = nc.tensor.matmul(down_ps[:, s, :], hT[:, fc, s * P:(s + 1) * P], w2[:, slot, fc, :],
                                                        start=(fc == 0), stop=(fc == FC - 1))
                        last.then_inc(down_ok, 1)
                    pe.wait_ge(y_ok, end)
                    pe.sem_inc(done, 1)

        @block.vector
        def _(dve):
            with dve.Fori(0, E // 2) as i:
                for slot in range(2):
                    e = i * 2 + slot
                    first, end = of_list(dve, 0, e), of_list(dve, 1, e)
                    dve.wait_ge(w_in[slot], i * 48 + 48)
                    settle(dve, m)
                    with dve.Fori(first, end) as b:
                        dve.wait_ge(down_ok, b + 1)
                        dve.wait_ge(y_out, b * 16 + 16)
                        dve.tensor_tensor(y[:], down_ps, b2[:, slot, None, :].broadcast_to([P, 2, D]), ALU.add).then_inc(y_ok, 1)


def combine(nc, m, a):
    with ExitStack() as ctx:
        def sb(name, shape, dt=F32):
            return ctx.enter_context(nc.sbuf_tensor(name, shape, dt))

        def sem(name):
            return ctx.enter_context(nc.semaphore(name))

        HALVES = ((0, 4), (4, 7))
        got = sb("got", [P, 7, 2, D])
        at = sb("at_c", [P, 7, 2], I32)
        z = sb("z", [P, 7, D])
        out = sb("out_c", [P, 7, D])
        st = sb("st_c", [P, 7, 6])
        mv = sb("mv_c", [P, 7, 2])
        var = sb("var_c", [P, 7])
        rs = sb("rs_c", [P, 7])
        nt = sb("nt_c", [P, 7])
        sd = sb("sd_c", [P, 7])
        back, at_ok, var_ok, sd_ok, z_ok, out_ok, out_sent = (
            [sem(f"{n}{k}") for k in range(2)]
            for n in ("back", "at_okc", "var_okc", "sd_okc", "z_okc", "out_okc", "out_sentc"))
        chain = sem("chain_c")
        out_v = a.out.rearrange("(t p) d -> p t d", p=P)
        block = ctx.enter_context(nc.Block())

        @block.gpsimd
        def _(pool):
            with pool.Fori(0, NT // 7) as g:
                for part, (j0, j1) in enumerate(HALVES):
                    pool.wait_ge(z_ok[part], g + 1)
                    settle(pool, m)
                    pool.tensor_copy(at[:, j0:j1, :], m.places[:, bass.ds(g * 7 + j0, j1 - j0), :]).then_inc(at_ok[part], 1)
                    pool.wait_ge(at_ok[part], g + 1)
                    settle(pool, m)
                    for j in range(j0, j1):
                        for k in range(2):
                            pool.indirect_dma_start(out=got[:, j, k, :], out_offset=None, in_=a.lists_out,
                                                    in_offset=bass.IndirectOffsetOnAxis(ap=at[:, j, k:k + 1], axis=0)
                                                    ).then_inc(back[part], 16)

        @block.vector
        def _(dve):
            for part in range(2):
                dve.sem_inc(z_ok[part], 1)

            def turn(g, first):
                c = Count(dve, chain, g * CHAIN_COMBINE, CHAIN_COMBINE)
                for part, (j0, j1) in enumerate(HALVES):
                    n = j1 - j0
                    dve.wait_ge(back[part], g * n * 32 + n * 32)
                    if not first:
                        dve.wait_ge(out_ok[part], g)
                    for j in range(j0, j1):
                        c.add(dve.scalar_tensor_tensor(z[:, j, :], got[:, j, 0, :], m.share[:, bass.ds(g * 7 + j, 1), 0:1].rearrange("p a b -> p (a b)"),
                                                       m.xn[:, bass.ds(g * 7 + j, 1), :].rearrange("p a b -> p (a b)"), ALU.mult, ALU.add))
                    c.wait()
                    for j in range(j0, j1):
                        last = dve.scalar_tensor_tensor(z[:, j, :], got[:, j, 1, :], m.share[:, bass.ds(g * 7 + j, 1), 1:2].rearrange("p a b -> p (a b)"),
                                                        z[:, j, :], ALU.mult, ALU.add)
                        if j == j1 - 1:
                            last.then_inc(z_ok[part], 1)
                    dve.wait_ge(z_ok[part], g + 2)
                    for j in range(j0, j1):
                        c.add(dve.bn_stats(st[:, j, :], z[:, j, :]))
                    c.wait()
                    settle(dve, m)
                    for j in range(j0, j1):
                        c.add(dve.bn_aggr(mv[:, j, :], st[:, j, :]))
                    c.wait()
                    dve.tensor_scalar(var[:, j0:j1], mv[:, j0:j1, 1], EPS, None, ALU.add).then_inc(var_ok[part], 1)
                    dve.wait_ge(sd_ok[part], g + 1)
                    r, v = rs[:, j0:j1], nt[:, j0:j1]
                    c.add(dve.reciprocal(r, sd[:, j0:j1]))
                    c.wait()
                    c.add(dve.tensor_tensor(v, r, r, ALU.mult))
                    c.wait()
                    c.add(dve.tensor_tensor(v, v, var[:, j0:j1], ALU.mult))
                    c.wait()
                    c.add(dve.tensor_scalar(v, v, -0.5, 1.5, ALU.mult, ALU.add))
                    c.wait()
                    c.add(dve.tensor_tensor(r, r, v, ALU.mult))
                    c.wait()
                    for j in range(j0, j1):
                        c.add(dve.tensor_scalar(z[:, j, :], z[:, j, :], mv[:, j, 0:1], rs[:, j:j + 1], ALU.subtract, ALU.mult))
                    c.wait()
                    wide = [P, n, D]
                    c.add(dve.tensor_tensor(z[:, j0:j1], z[:, j0:j1], m.vecs[:, None, V_FGAMMA:V_FGAMMA + D].broadcast_to(wide), ALU.mult))
                    c.wait()
                    c.add(dve.tensor_tensor(z[:, j0:j1], z[:, j0:j1], m.vecs[:, None, V_FBETA:V_FBETA + D].broadcast_to(wide), ALU.add))
                    c.wait()
                    if not first:
                        dve.wait_ge(out_sent[part], g * 16)
                    dve.tensor_tensor(out[:, j0:j1], z[:, j0:j1], m.x1[:, bass.ds(g * 7 + j0, n), :], ALU.add).then_inc(out_ok[part], 1)
                c.end()

            turn(0, True)
            with dve.Fori(1, NT // 7) as g:
                turn(g, False)

        @block.scalar
        def _(act):
            with act.Fori(0, NT // 7) as g:
                for part, (j0, j1) in enumerate(HALVES):
                    act.wait_ge(var_ok[part], g + 1)
                    act.activation(sd[:, j0:j1], var[:, j0:j1], ACT.Sqrt).then_inc(sd_ok[part], 1)

        @block.sync
        def _(sp):
            with sp.Fori(0, NT // 7) as g:
                for part, (j0, j1) in enumerate(HALVES):
                    sp.wait_ge(out_ok[part], g + 1)
                    sp.dma_start(out_v[:, bass.ds(g * 7 + j0, j1 - j0), :], out[:, j0:j1, :]).then_inc(out_sent[part], 16)
            for part in range(2):
                sp.wait_ge(out_sent[part], NT // 7 * 16)


def build_program(nc, a):
    with ExitStack() as ctx:
        m = memory(nc, ctx)
        prepare(nc, m, a)
        regroup(nc, m, a)
        layers(nc, m, a)
        route(nc, m, a)
        experts(nc, m, a)
        combine(nc, m, a)


def lay_out(x, src, dst, edge_weight, L0_gnn_W, L0_gnn_b, L0_gnn_gamma, L0_gnn_beta, L0_mix_Wq, L0_mix_Wkv,
            L0_mix_Wproj, L0_mix_bproj, L0_ffn_gate_w, L0_ffn_gate_b, L0_ffn_w1, L0_ffn_b1, L0_ffn_w2, L0_ffn_b2,
            L0_ffn_gamma, L0_ffn_beta):
    f = np.float32

    def padded(v, n, fill=0):
        out = np.full((n,) + v.shape[1:], fill, v.dtype)
        out[:v.shape[0]] = v
        return out

    def rows(w):
        return w.reshape(DC, P, -1).transpose(1, 0, 2)

    const = np.zeros((P, C_N), f)
    const[:, C_ID:C_ID + P] = np.eye(P)
    const[:, C_TRI:C_TRI + P] = np.triu(np.ones((P, P)), 1)
    const[:, C_IOTA:C_IOTA + P] = np.arange(P)
    const[:, C_ONE:C_ONE + P] = 1
    const[:, C_VALID:C_VALID + NT] = (np.arange(P)[:, None] + P * np.arange(NT)) < N
    const[:, C_POW] = -0.5
    const[:, C_DOWN:C_DOWN + E] = E - np.arange(E)
    const[:, C_TILE:C_TILE + NT] = P * np.arange(NT)
    vecs = np.concatenate([L0_gnn_b, L0_gnn_gamma, L0_gnn_beta, L0_mix_bproj, L0_ffn_gamma, L0_ffn_beta, L0_ffn_gate_b])
    weights = np.concatenate([rows(L0_mix_Wkv.T), rows(L0_mix_Wq.T), rows(L0_mix_Wproj.T), rows(L0_gnn_W),
                              rows(L0_ffn_gate_w)], axis=2)
    src_b = padded(src, NEP).reshape(NB, P)
    dst_b = padded(dst, NEP, NP - 1).reshape(NB, P)
    w_b = padded(edge_weight, NEP).reshape(NB, P)
    dst_next = padded(dst[1:], NEP, NP - 1)
    return dict(
        x=padded(x, NP), const=const, vecs=np.tile(vecs, (P, 1)), weights=weights,
        src_cols=src_b.T, dst_cols=dst_b.T, w_cols=w_b.T,
        dst_seq=np.stack([dst_b.reshape(NB // 7, 7 * P), dst_next.reshape(NB // 7, 7 * P)], axis=1),
        w1=L0_ffn_w1, w2=L0_ffn_w2, b1=L0_ffn_b1.reshape(E, FC, P).transpose(2, 1, 0),
        b2=np.broadcast_to(L0_ffn_b2[:, None, :], (E, P, D)),
    )


def kernel(**inputs):
    import concourse.bacc as bacc
    from concourse.bass_utils import run_bass_kernel_spmd

    nc = bacc.Bacc("TRN2", target_bir_lowering=False, num_devices=1)
    arrays, a = {}, Names()
    for name, v in lay_out(**{k: np.asarray(v) for k, v in inputs.items()}).items():
        v = np.ascontiguousarray(v)
        arrays["in_" + name] = v
        a.__dict__[name] = nc.dram_tensor("in_" + name, v.shape, mybir.dt.from_np(v.dtype), kind="ExternalInput").ap()
    a.table = nc.dram_tensor("table", (NP, D), F32).ap()
    a.edges = nc.dram_tensor("edges", (NEP, 3), F32).ap()
    a.lists_in = nc.dram_tensor("lists_in", (BLOCKS * BLOCK, D), F32).ap()
    a.lists_out = nc.dram_tensor("lists_out", (BLOCKS * BLOCK, D), F32).ap()
    a.out = nc.dram_tensor("out", (NP, D), F32, kind="ExternalOutput").ap()
    build_program(nc, a)
    r = run_bass_kernel_spmd(nc, [arrays], core_ids=[0])
    return r.results[0]["out"][:N]
```
